# Optimizing a Trainium2 kernel written in Bass

```python
import numpy as np
import jax
import jax.numpy as jnp

def _softmax(x, axis=-1):
    return jax.nn.softmax(x, axis=axis)

def _gelu(x):
    return jax.nn.gelu(x, approximate=True)

def _silu(x):
    return jax.nn.silu(x)

def _sigmoid(x):
    return jax.nn.sigmoid(x)

def _layernorm(x, axis=-1, eps=1e-05):
    m = jnp.mean(x, axis=axis, keepdims=True)
    v = jnp.var(x, axis=axis, keepdims=True)
    return (x - m) / jnp.sqrt(v + eps)

def _scatter_add(tgt, idx, src, axis=0):
    return tgt.at[idx].add(src)

def _segment_sum(src, seg, n):
    return jax.ops.segment_sum(src, seg, n)
kernel_name = 'mk_adj_preln_d1_adj_r2_351932'

def setup_inputs(seed: int=0):
    np.random.seed(seed)
    _w = jnp.asarray

    def _rec_inputs():
        import jax
        import jax.numpy as jnp
        _gk = jax.random.key(seed)
        x = 0.0001732 + 1 * jax.random.normal(jax.random.fold_in(_gk, 1), (5120, 64), jnp.float32)
        _w = (1.0 + jnp.arange(5120, dtype=jnp.float32)) ** (-0.5)
        _w = _w / _w.mean()
        _pij = jnp.clip(0.00078125 * _w[:, None] * _w[None, :], 0.0, 1.0)
        _a = jax.random.uniform(jax.random.fold_in(_gk, 2), (5120, 5120)) < _pij
        _af = _a.astype(jnp.float32)
        _af = _af * jax.random.uniform(jax.random.fold_in(_gk, 3), (5120, 5120), jnp.float32, 0.05, 0.02)
        adj = _af
        return (x, adj)
    x, adj = _rec_inputs()

    def _L0_gnn_setup():
        import jax, jax.numpy as jnp
        import numpy as np
        N_USERS = 2048
        N_ITEMS = 3072
        EMB = 64
        LN_EPS = 1e-05
        key = jax.random.key(seed)
        ks = jax.random.split(key, 10)
        N = N_USERS + N_ITEMS
        ego = jax.random.normal(ks[0], (N, EMB), jnp.float32)
        adj = (jax.random.uniform(ks[1], (N, N), jnp.float32) < 0.01).astype(jnp.float32) * 0.02
        xav = float(np.sqrt(6.0 / (EMB + EMB)))
        W_u = jax.random.uniform(ks[2], (EMB, EMB), jnp.float32, -xav, xav)
        W_i = jax.random.uniform(ks[3], (EMB, EMB), jnp.float32, -xav, xav)
        diag_u = jax.random.uniform(ks[4], (N_USERS,), jnp.float32, 0.99, 1.01)
        diag_i = jax.random.uniform(ks[5], (N_ITEMS,), jnp.float32, 0.99, 1.01)
        par_u = jax.random.uniform(ks[6], (2,), jnp.float32, 0.0, 0.99)
        par_i = jax.random.uniform(ks[7], (2,), jnp.float32, 0.0, 0.99)
        ln_gamma = jnp.ones((EMB,), jnp.float32)
        ln_beta = jnp.zeros((EMB,), jnp.float32)
        return {'ego_embeddings': ego, 'adj': adj, 'W_u': W_u, 'diag_u': diag_u, 'par_u': par_u, 'W_i': W_i, 'diag_i': diag_i, 'par_i': par_i, 'ln_gamma': ln_gamma, 'ln_beta': ln_beta}
    _L0_gnn_all = _L0_gnn_setup()
    _L0_gnn_in = {k: v for k, v in _L0_gnn_all.items() if k in ('W_u', 'diag_u', 'par_u', 'W_i', 'diag_i', 'par_i', 'ln_gamma', 'ln_beta')}
    del _L0_gnn_all
    return {'x': x, 'adj': adj, 'L0_gnn_W_u': _L0_gnn_in['W_u'], 'L0_gnn_diag_u': _L0_gnn_in['diag_u'], 'L0_gnn_par_u': _L0_gnn_in['par_u'], 'L0_gnn_W_i': _L0_gnn_in['W_i'], 'L0_gnn_diag_i': _L0_gnn_in['diag_i'], 'L0_gnn_par_i': _L0_gnn_in['par_i'], 'L0_gnn_ln_gamma': _L0_gnn_in['ln_gamma'], 'L0_gnn_ln_beta': _L0_gnn_in['ln_beta']}

def reference(x, adj, L0_gnn_W_u, L0_gnn_diag_u, L0_gnn_par_u, L0_gnn_W_i, L0_gnn_diag_i, L0_gnn_par_i, L0_gnn_ln_gamma, L0_gnn_ln_beta):
    import jax
    import jax.numpy as jnp

    def _L0_gnn_ref(ego_embeddings, adj, W_u, diag_u, par_u, W_i, diag_i, par_i, ln_gamma, ln_beta):
        import jax, jax.numpy as jnp
        import numpy as np
        N_USERS = 2048
        N_ITEMS = 3072
        EMB = 64
        LN_EPS = 1e-05
        nu = diag_u.shape[0]
        res = ego_embeddings
        ego_u = ego_embeddings[:nu]
        ego_i = ego_embeddings[nu:]
        u = par_u[0] * par_u[1] * (diag_u[:, None] * ego_u @ W_u) + ego_u
        i = par_i[0] * par_i[1] * (diag_i[:, None] * ego_i @ W_i) + ego_i
        e = jnp.concatenate([u, i], axis=0)
        h = adj @ (adj.T @ e)
        mu = jnp.mean(h, axis=-1, keepdims=True)
        var = jnp.var(h, axis=-1, keepdims=True)
        out = (h - mu) * jax.lax.rsqrt(var + LN_EPS) * ln_gamma + ln_beta + res
        return out
    h = jnp.maximum(_layernorm(x, axis=-1), 0.0)
    x = x + _L0_gnn_ref(h, adj, L0_gnn_W_u, L0_gnn_diag_u, L0_gnn_par_u, L0_gnn_W_i, L0_gnn_diag_i, L0_gnn_par_i, L0_gnn_ln_gamma, L0_gnn_ln_beta)
    return x

_drawn_inputs = setup_inputs


def setup_inputs(seed=0):
    import zlib

    import numpy as np

    out = dict(_drawn_inputs(seed))
    spreads = {'L0_gnn_ln_gamma': (1.0, 0.2), 'L0_gnn_ln_beta': (0.0, 0.1)}
    factors = {'L0_gnn_diag_u': 8.0, 'L0_gnn_W_i': 2.924, 'L0_gnn_diag_i': 8.0}
    for name, (base, spread) in spreads.items():
        noise = np.random.default_rng([zlib.crc32(name.encode()), seed]).standard_normal(out[name].shape)
        drawn = base * np.exp(spread * noise) if base else spread * noise
        out[name] = jnp.asarray(drawn.astype(out[name].dtype))
    for name, factor in factors.items():
        out[name] = (out[name] * factor).astype(out[name].dtype)
    return out
```

```python
from contextlib import ExitStack

import concourse.bass as bass
from concourse import mybir

P = 128
N = 5120
D = 64
N_USERS = 2048
CHUNK = 512
PANELS = N // CHUNK
BLOCKS = CHUNK // P
GROUPS = N // (2 * CHUNK)
GT = 2 * BLOCKS
TILES = N // P
USER_GROUPS = N_USERS // (2 * CHUNK)
LN_EPS = 1e-5

F32 = mybir.dt.float32
ALU = mybir.AluOpType
ACT = mybir.ActivationFunctionType
AX = mybir.AxisListType


def gnn_layer(nc, x, adj_rows, adj_cols, w_u, w_i, diag, par_u, par_i, gamma, beta, out):
    ctx = ExitStack()
    with ctx:
        def sb(name, shape):
            return ctx.enter_context(nc.sbuf_tensor(name, shape, F32))

        def sem(name):
            return ctx.enter_context(nc.semaphore(name))

        turned = sb("turned", [P, 2, GROUPS, BLOCKS, CHUNK])
        direct = sb("direct", [P, GROUPS, BLOCKS, CHUNK])
        cols = sb("cols", [P, GROUPS, BLOCKS, CHUNK])

        xs = sb("xs", [P, TILES, D])
        e = sb("e", [P, TILES, D])
        ident = sb("ident", [P, P])
        wdiag = sb("wdiag", [P, 2, P])
        diag_s = sb("diag_s", [P, TILES])
        par = sb("par", [P, 2, 2])
        gamma_s = sb("gamma_s", [P, D])
        beta_s = sb("beta_s", [P, D])
        eps = sb("eps", [P, 1])
        centred = sb("centred", [P, 2, GT, D])
        squares = sb("squares", [P, 2, GT, D])
        scaled = sb("scaled", [P, 2, GT, D])
        mean = sb("mean", [P, 2, GT])
        var = sb("var", [P, 2, GT])
        rstd = sb("rstd", [P, 2, GT])
        across = sb("across", [P, 2, CHUNK])
        t_across = sb("t_across", [P, CHUNK])
        t = sb("t", [P, 2, BLOCKS, D])

        h_acc = ctx.enter_context(nc.psum_tensor("h_acc", [P, GROUPS, CHUNK], F32))
        t_acc = ctx.enter_context(nc.psum_tensor("t_acc", [P, CHUNK], F32))
        turn = ctx.enter_context(nc.psum_tensor("turn", [P, 2, CHUNK], F32))

        s_x = [sem(f"s_x{m}") for m in range(GROUPS)]
        s_diag = sem("s_diag")
        s_vectors = sem("s_vectors")
        s_w = sem("s_w")
        s_turned = [[sem(f"s_turned{a}{m}") for m in range(GROUPS)] for a in range(2)]
        s_direct = [sem(f"s_direct{m}") for m in range(GROUPS)]
        s_cols = [sem(f"s_cols{m}") for m in range(GROUPS)]
        s_eps = sem("s_eps")
        s_zero = sem("s_zero")
        s_ident = sem("s_ident")
        s_sum = sem("s_sum")
        s_mean = sem("s_mean")
        s_centred = sem("s_centred")
        s_squares = sem("s_squares")
        s_var = sem("s_var")
        s_std = sem("s_std")
        s_rstd = sem("s_rstd")
        s_scale = sem("s_scale")
        s_h = sem("s_h")
        s_h_across = sem("s_h_across")
        s_h_copied = sem("s_h_copied")
        s_hw = sem("s_hw")
        s_hw_copied = sem("s_hw_copied")
        s_hw_back = sem("s_hw_back")
        s_dhw = sem("s_dhw")
        s_e = sem("s_e")
        s_res = sem("s_res")
        s_res_part = sem("s_res_part")
        s_first_done = sem("s_first_done")
        s_second_done = sem("s_second_done")
        s_turn_full = [sem(f"s_turn_full{b}") for b in range(2)]
        s_turn_kept = [sem(f"s_turn_kept{b}") for b in range(2)]
        s_t_across = sem("s_t_across")
        s_t_back = sem("s_t_back")
        s_t = sem("s_t")
        s_o_across = sem("s_o_across")
        s_o_back = sem("s_o_back")
        s_o_gamma = sem("s_o_gamma")
        s_o_scaled = sem("s_o_scaled")
        s_o_done = sem("s_o_done")
        s_out = sem("s_out")

        TURNS = GROUPS * BLOCKS // 2

        def steps(eng, step):
            step(0, 0, 0)
            step(1, 1, 0)
            with eng.Fori(0, PANELS // 2 - 1) as i:
                step(2 * i + 2, 0, i + 1)
                step(2 * i + 3, 1, i + 1)
            step(PANELS, 0, PANELS // 2)

        def has_first(g):
            return not (isinstance(g, int) and g == PANELS)

        def has_second(g):
            return not (isinstance(g, int) and g == 0)

        def wait_count(eng, s, count):
            if not (isinstance(count, int) and count <= 0):
                eng.wait_ge(s, count)

        block = ctx.enter_context(nc.Block())

        @block.sync
        def _(sp):
            sp.dma_start(xs[:, 0:GT, :], x[:, 0:GT, :]).then_inc(s_x[0], 16)
            sp.dma_start(diag_s[:], diag).then_inc(s_diag, 16)
            for n, v in enumerate((par_u, par_i)):
                sp.dma_start(par[:, n, :], v.partition_broadcast(P)).then_inc(s_diag, 16)

            def step(g, a, half):
                for m in range(GROUPS):
                    if has_first(g):
                        if not isinstance(g, int) or g >= 2:
                            sp.wait_ge(s_second_done, GROUPS * (g - 2) + m + 1)
                        sp.dma_start(turned[:, a, m].rearrange("p b c -> p (b c)"),
                                     adj_rows[g, m, 0]).then_inc(s_turned[a][m], 16)
                        if has_second(g):
                            sp.wait_ge(s_first_done, GROUPS * (g - 1) + m + 1)
                        sp.dma_start(direct[:, m].rearrange("p b c -> p (b c)"),
                                     adj_rows[g, m, 1]).then_inc(s_direct[m], 16)
                    if has_second(g):
                        if not isinstance(g, int) or g >= 2:
                            sp.wait_ge(s_second_done, GROUPS * (g - 2) + m + 1)
                        sp.dma_start(cols[:, m].rearrange("p b c -> p (b c)"),
                                     adj_cols[g - 1, m]).then_inc(s_cols[m], 16)

            steps(sp, step)
            for m in range(GROUPS):
                sp.wait_ge(s_o_done, m + 1)
                sp.dma_start(out[:, GT * m:GT * (m + 1), :], xs[:, GT * m:GT * (m + 1), :]).then_inc(s_out, 16)
            sp.wait_ge(s_out, 16 * GROUPS)

        @block.gpsimd
        def _(pool):
            nc.gpsimd.memset(eps[:], LN_EPS).then_inc(s_eps, 1)
            nc.gpsimd.memset(ident[:], 0.0).then_inc(s_zero, 1)
            nc.gpsimd.memset(wdiag[:], 0.0).then_inc(s_zero, 1)
            pool.wait_ge(s_zero, 1)
            nc.gpsimd.affine_select(out=ident[:], in_=ident[:], compare_op=ALU.not_equal, fill=1.0, base=0,
                                    pattern=[[-1, P]], channel_multiplier=1).then_inc(s_ident, 1)
            pool.wait_ge(s_vectors, 32)
            for m in range(GROUPS):
                tiles = slice(GT * m, GT * (m + 1))
                pool.wait_ge(s_x[m], 16)
                pool.wait_ge(s_centred, m + 1)
                nc.gpsimd.tensor_tensor(xs[:, tiles, :], xs[:, tiles, :],
                                        beta_s[:].unsqueeze(1).to_broadcast([P, GT, D]),
                                        ALU.add).then_inc(s_res_part, 1)
                pool.wait_ge(s_res_part, m + 1)
                pool.wait_ge(s_h, m + 1)
                nc.gpsimd.tensor_tensor(xs[:, tiles, :], xs[:, tiles, :], e[:, tiles, :], ALU.add).then_inc(s_res, 1)
            for m in range(GROUPS):
                n = GROUPS + m
                pool.wait_ge(s_centred, n + 1)
                if m >= 2:
                    pool.wait_ge(s_o_scaled, m - 1)
                nc.gpsimd.tensor_tensor(scaled[:, n % 2], centred[:, n % 2],
                                        gamma_s[:].unsqueeze(1).to_broadcast([P, GT, D]),
                                        ALU.mult).then_inc(s_o_gamma, 1)

        @block.scalar
        def _(act):
            for m in range(1, GROUPS):
                act.dma_start(xs[:, GT * m:GT * (m + 1), :], x[:, GT * m:GT * (m + 1), :]).then_inc(s_x[m], 16)
            act.wait_ge(s_zero, 2)
            for n, w in enumerate((w_u, w_i)):
                for d in range(2):
                    act.dma_start(wdiag[D * d:D * (d + 1), n, D * d:D * (d + 1)], w).then_inc(s_w, 16)
            act.dma_start(gamma_s[:], gamma.partition_broadcast(P)).then_inc(s_vectors, 16)
            act.dma_start(beta_s[:], beta.partition_broadcast(P)).then_inc(s_vectors, 16)

            def square(n):
                act.wait_ge(s_centred, n + 1)
                if n >= 2:
                    act.wait_ge(s_var, n - 1)
                nc.scalar.activation(squares[:, n % 2], centred[:, n % 2], ACT.Square).then_inc(s_squares, 1)

            def std(n):
                act.wait_ge(s_var, n + 1)
                if n == 0:
                    act.wait_ge(s_eps, 1)
                nc.scalar.activation(var[:, n % 2], var[:, n % 2], ACT.Sqrt, bias=eps[:],
                                     scale=1.0 / D).then_inc(s_std, 1)

            def h_across(m):
                act.wait_ge(s_h_across, m + 1)
                if m >= 2:
                    act.wait_ge(s_hw_back, m - 1)
                nc.scalar.copy(across[:, m % 2], h_acc[:, m]).then_inc(s_h_copied, 1)

            def hw_across(m):
                act.wait_ge(s_hw, m + 1)
                nc.scalar.copy(across[:, m % 2], h_acc[:, m]).then_inc(s_hw_copied, 1)

            def step(g, a, half):
                for m in range(GROUPS):
                    if isinstance(g, int) and g == 0 and m + 1 < GROUPS:
                        layer_input(m + 1)
                    if has_first(g):
                        if m == GROUPS - 1:
                            act.wait_ge(s_first_done, GROUPS * (g + 1))
                            nc.scalar.copy(t_across[:], t_acc[:]).then_inc(s_t_across, 1)
                        for b in range(1, BLOCKS, 2):
                            act.wait_ge(s_turn_full[1], TURNS * g + 2 * m + b // 2 + 1)
                            nc.scalar.copy(turned[:, a, m, :, P * b:P * (b + 1)],
                                           turn[:, 1].rearrange("p (k r) -> p k r", k=BLOCKS)
                                           ).then_inc(s_turn_kept[1], 1)

            def layer_input(m):
                square(m)
                std(m)
                h_across(m)
                hw_across(m)

            layer_input(0)
            steps(act, step)
            for m in range(GROUPS):
                act.wait_ge(s_second_done, GROUPS * (PANELS - 1) + m + 1)
                if m >= 2:
                    act.wait_ge(s_o_back, m - 1)
                nc.scalar.copy(across[:, m % 2], h_acc[:, m]).then_inc(s_o_across, 1)
                square(GROUPS + m)
                std(GROUPS + m)

        @block.vector
        def _(dve):
            def normalise(n, source):
                nc.vector.tensor_reduce(mean[:, n % 2], source, AX.X, ALU.add).then_inc(s_sum, 1)
                dve.wait_ge(s_sum, n + 1)
                nc.vector.tensor_scalar(mean[:, n % 2], mean[:, n % 2], 1.0 / D, None, ALU.mult).then_inc(s_mean, 1)
                dve.wait_ge(s_mean, n + 1)
                nc.vector.tensor_tensor(centred[:, n % 2], source,
                                        mean[:, n % 2].unsqueeze(2).to_broadcast([P, GT, D]),
                                        ALU.subtract).then_inc(s_centred, 1)

            def variance(n):
                dve.wait_ge(s_squares, n + 1)
                nc.vector.tensor_reduce(var[:, n % 2], squares[:, n % 2], AX.X, ALU.add).then_inc(s_var, 1)
                dve.wait_ge(s_std, n + 1)
                nc.vector.reciprocal(rstd[:, n % 2], var[:, n % 2]).then_inc(s_rstd, 1)
                dve.wait_ge(s_rstd, n + 1)
                return rstd[:, n % 2].unsqueeze(2).to_broadcast([P, GT, D])

            def layer_input(m):
                dve.wait_ge(s_x[m], 16)
                normalise(m, xs[:, GT * m:GT * (m + 1), :])
                r = variance(m)
                nc.vector.scalar_tensor_tensor(e[:, GT * m:GT * (m + 1), :], centred[:, m % 2], 0.0, r,
                                               ALU.max, ALU.mult).then_inc(s_h, 1)

            def embed(m):
                tiles = slice(GT * m, GT * (m + 1))
                dve.wait_ge(s_hw_back, m + 1)
                nc.vector.tensor_tensor(scaled[:, m % 2], h_acc[:, m].rearrange("p (k d) -> p k d", d=D),
                                        diag_s[:, tiles].unsqueeze(2).to_broadcast([P, GT, D]),
                                        ALU.mult).then_inc(s_dhw, 1)
                dve.wait_ge(s_dhw, m + 1)
                dve.wait_ge(s_res, m + 1)
                nc.vector.tensor_tensor(e[:, tiles, :], scaled[:, m % 2], e[:, tiles, :], ALU.add).then_inc(s_e, 1)

            def keep_turn(g, a, m, b):
                dve.wait_ge(s_turn_full[0], TURNS * g + 2 * m + b // 2 + 1)
                nc.vector.tensor_copy(turned[:, a, m, :, P * b:P * (b + 1)],
                                      turn[:, 0].rearrange("p (k r) -> p k r", k=BLOCKS)
                                      ).then_inc(s_turn_kept[0], 1)

            def step(g, a, half):
                for m in range(GROUPS):
                    if has_first(g):
                        prologue = isinstance(g, int) and g == 0 and m + 1 < GROUPS
                        if prologue:
                            layer_input(m + 1)
                        keep_turn(g, a, m, 0)
                        if prologue:
                            embed(m + 1)
                        if m == GROUPS - 1:
                            dve.wait_ge(s_t_back, g + 1)
                            nc.vector.tensor_reduce(t[:, a],
                                                    t_acc[:].rearrange("p (b s d) -> p b d s", b=BLOCKS, s=2),
                                                    AX.X, ALU.add).then_inc(s_t, 1)
                        keep_turn(g, a, m, 2)

            layer_input(0)
            dve.wait_ge(s_diag, 48)
            for n, (lo, hi) in enumerate(((0, N_USERS // P), (N_USERS // P, TILES))):
                nc.vector.tensor_scalar(diag_s[:, lo:hi], diag_s[:, lo:hi], par[:, n, 0:1], par[:, n, 1:2],
                                        ALU.mult, ALU.mult).then_inc(s_scale, 1)
            dve.wait_ge(s_scale, 2)
            embed(0)
            steps(dve, step)
            for m in range(GROUPS):
                n = GROUPS + m
                dve.wait_ge(s_o_back, m + 1)
                normalise(n, turn[:, m % 2].rearrange("p (k d) -> p k d", d=D))
                r = variance(n)
                dve.wait_ge(s_o_gamma, m + 1)
                nc.vector.tensor_tensor(scaled[:, n % 2], scaled[:, n % 2], r, ALU.mult).then_inc(s_o_scaled, 1)
                dve.wait_ge(s_o_scaled, m + 1)
                dve.wait_ge(s_res, GROUPS)
                res = xs[:, GT * m:GT * (m + 1), :].rearrange("p (s b) d -> p b s d", s=2)
                nc.vector.tensor_tensor(res, scaled[:, n % 2].rearrange("p (b s) d -> p b s d", s=2), res,
                                        ALU.add).then_inc(s_o_done, 1)

        @block.tensor
        def _(pe):
            def h_turn(m):
                if m == 0:
                    pe.wait_ge(s_ident, 1)
                pe.wait_ge(s_h, m + 1)
                for b in range(BLOCKS):
                    last = nc.tensor.transpose(h_acc[:, m, P * b:P * (b + 1)],
                                               e[:, GT * m + 2 * b:GT * m + 2 * b + 2, :]
                                               .rearrange("p k d -> p (k d)"), ident[:])
                last.then_inc(s_h_across, 1)

            def h_weights(m):
                if m == 0:
                    pe.wait_ge(s_w, 64)
                pe.wait_ge(s_h_copied, m + 1)
                nc.tensor.matmul(h_acc[:, m], wdiag[:, int(m >= USER_GROUPS)], across[:, m % 2],
                                 start=True, stop=True).then_inc(s_hw, 1)

            def hw_turn(m):
                pe.wait_ge(s_hw_copied, m + 1)
                for b in range(BLOCKS):
                    last = nc.tensor.transpose(h_acc[:, m, P * b:P * (b + 1)],
                                               across[:, m % 2, P * b:P * (b + 1)], ident[:])
                last.then_inc(s_hw_back, 1)

            def first(g, a, half, m):
                pe.wait_ge(s_turned[a][m], 16 * (half + 1))
                pe.wait_ge(s_direct[m], 16 * (g + 1))
                if isinstance(g, int) and g == 0:
                    pe.wait_ge(s_e, m + 1)
                if m == 0 and has_second(g):
                    pe.wait_ge(s_t, g)
                for k in range(BLOCKS):
                    for s, rows in enumerate((turned[:, a, m, k], direct[:, m, k])):
                        last = nc.tensor.matmul(t_acc[D * s:D * (s + 1), :], e[:, GT * m + BLOCKS * s + k, :], rows,
                                                start=(m == 0 and k == 0),
                                                stop=(m == GROUPS - 1 and k == BLOCKS - 1))
                last.then_inc(s_first_done, 1)

            def turn_block(g, a, m, b):
                wait_count(pe, s_turn_kept[b % 2], TURNS * g + 2 * m + b // 2)
                for k in range(BLOCKS):
                    last = nc.tensor.transpose(turn[:, b % 2, P * k:P * (k + 1)],
                                               turned[:, a, m, k, P * b:P * (b + 1)], ident[:])
                last.then_inc(s_turn_full[b % 2], 1)

            def second(g, a, half, m, blocks):
                if blocks[0] == 0:
                    pe.wait_ge(s_cols[m], 16 * g)
                    for b in range(2):
                        pe.wait_ge(s_turn_kept[b], TURNS * (g - 1) + 2 * m + 2)
                    if m == 0:
                        pe.wait_ge(s_t, g)
                for b in blocks:
                    for s, rows in enumerate((turned[:, 1 - a, m, :, P * b:P * (b + 1)], cols[:, m, b])):
                        last = nc.tensor.matmul(h_acc[D * s:D * (s + 1), m], t[:, 1 - a, b, :], rows,
                                                start=(isinstance(g, int) and g == 1 and b == 0),
                                                stop=(isinstance(g, int) and g == PANELS and b == BLOCKS - 1),
                                                skip_group_check=True)
                if blocks[-1] == BLOCKS - 1:
                    last.then_inc(s_second_done, 1)

            def t_turn(g):
                pe.wait_ge(s_t_across, g + 1)
                for b in range(BLOCKS):
                    last = nc.tensor.transpose(t_acc[:, P * b:P * (b + 1)], t_across[:, P * b:P * (b + 1)], ident[:])
                last.then_inc(s_t_back, 1)

            def step(g, a, half):
                for m in range(GROUPS):
                    prologue = isinstance(g, int) and g == 0 and m + 1 < GROUPS
                    if has_first(g):
                        first(g, a, half, m)
                        if prologue:
                            h_turn(m + 1)
                        turn_block(g, a, m, 0)
                        if prologue:
                            h_weights(m + 1)
                        turn_block(g, a, m, 1)
                        if prologue:
                            hw_turn(m + 1)
                    if has_second(g):
                        second(g, a, half, m, (0, 1))
                    if has_first(g):
                        if m == GROUPS - 1:
                            t_turn(g)
                        turn_block(g, a, m, 2)
                        turn_block(g, a, m, 3)
                    if has_second(g):
                        second(g, a, half, m, (2, 3))
                    if not has_first(g) and m >= 1:
                        out_turn(m - 1)

            def out_turn(m):
                pe.wait_ge(s_o_across, m + 1)
                if m >= 2:
                    pe.wait_ge(s_centred, GROUPS + m - 1)
                else:
                    pe.wait_ge(s_turn_kept[m], TURNS * PANELS)
                for b in range(BLOCKS):
                    last = nc.tensor.transpose(turn[:, m % 2, P * b:P * (b + 1)],
                                               across[:, m % 2, P * b:P * (b + 1)], ident[:])
                last.then_inc(s_o_back, 1)

            h_turn(0)
            h_weights(0)
            hw_turn(0)
            steps(pe, step)
            out_turn(GROUPS - 1)


def kernel(x, adj, L0_gnn_W_u, L0_gnn_diag_u, L0_gnn_par_u, L0_gnn_W_i, L0_gnn_diag_i, L0_gnn_par_i,
           L0_gnn_ln_gamma, L0_gnn_ln_beta):
    import concourse.bacc as bacc
    import numpy as np
    from concourse.bass_utils import run_bass_kernel_spmd

    def tiles(v):
        v = np.asarray(v)
        return np.ascontiguousarray(np.swapaxes(v.reshape(TILES, P, *v.shape[1:]), 0, 1))

    by_rows = np.asarray(adj).reshape(GROUPS, 2, BLOCKS, P, PANELS, CHUNK)
    by_cols = np.asarray(adj).reshape(GROUPS, 2, CHUNK, PANELS, BLOCKS, P)[:, 1]
    arrays = {
        "x": tiles(x),
        "adj_rows": np.ascontiguousarray(by_rows.transpose(4, 0, 1, 3, 2, 5)).reshape(
            PANELS, GROUPS, 2, P, BLOCKS * CHUNK),
        "adj_cols": np.ascontiguousarray(by_cols.transpose(2, 0, 4, 3, 1)).reshape(
            PANELS, GROUPS, P, BLOCKS * CHUNK),
        "w_u": np.asarray(L0_gnn_W_u),
        "w_i": np.asarray(L0_gnn_W_i),
        "diag": tiles(np.concatenate([np.asarray(L0_gnn_diag_u), np.asarray(L0_gnn_diag_i)])),
        "par_u": np.asarray(L0_gnn_par_u),
        "par_i": np.asarray(L0_gnn_par_i),
        "gamma": np.asarray(L0_gnn_ln_gamma),
        "beta": np.asarray(L0_gnn_ln_beta),
    }
    nc = bacc.Bacc("TRN2", target_bir_lowering=False, num_devices=1)
    ins = [nc.dram_tensor(name, a.shape, F32, kind="ExternalInput").ap() for name, a in arrays.items()]
    out = nc.dram_tensor("out", (P, TILES, D), F32, kind="ExternalOutput").ap()
    gnn_layer(nc, *ins, out)
    got = run_bass_kernel_spmd(nc, [arrays], core_ids=[0]).results[0]["out"]
    return np.ascontiguousarray(np.swapaxes(got, 0, 1)).reshape(N, D)
```

```python
from contextlib import ExitStack

import concourse.bass as bass
from concourse import mybir

P = 128
N = 5120
D = 64
N_USERS = 2048
CHUNK = 512
PANELS = N // CHUNK
BLOCKS = CHUNK // P
GROUPS = N // (2 * CHUNK)
GT = 2 * BLOCKS
TILES = N // P
USER_GROUPS = N_USERS // (2 * CHUNK)
TURNS = GROUPS * BLOCKS // 2
FIRST_BOTH = ()
LAST = PANELS - 1
LAST_LOADED = (0, 1, 2, 3, 4)
LAST_TURNED = [m for m in range(GROUPS) if m not in LAST_LOADED]
LN_EPS = 1e-5

F32 = mybir.dt.float32
BF16 = mybir.dt.bfloat16
ALU = mybir.AluOpType
ACT = mybir.ActivationFunctionType
AX = mybir.AxisListType


def gnn_layer(nc, x, adj_rows, adj_cols, adj_last, w_u, w_i, diag, par_u, par_i, gamma, beta, out):
    ctx = ExitStack()
    with ctx:
        def sb(name, shape):
            return ctx.enter_context(nc.sbuf_tensor(name, shape, F32))

        def sem(name):
            return ctx.enter_context(nc.semaphore(name))

        turned = sb("turned", [P, 2, GROUPS, BLOCKS, CHUNK])
        direct = sb("direct", [P, GROUPS, BLOCKS, CHUNK])
        cols = sb("cols", [P, GROUPS, BLOCKS, CHUNK])

        xs = sb("xs", [P, TILES, D])
        e = sb("e", [P, TILES, D])
        ident = sb("ident", [P, P])
        centre = sb("centre", [P, P])
        wdiag = sb("wdiag", [P, 2, P])
        diag_s = sb("diag_s", [P, TILES])
        par = sb("par", [P, 2, 2])
        gamma_s = sb("gamma_s", [P, D])
        beta_s = sb("beta_s", [P, D])
        eps = sb("eps", [P, 1])
        centred = sb("centred", [P, 2, GT, D])
        squares = sb("squares", [P, 2, GT, D])
        scaled = sb("scaled", [P, 2, GT, D])
        mean = sb("mean", [P, 2, GT])
        var = sb("var", [P, 2, GT])
        rstd = sb("rstd", [P, 2, GT])
        across = sb("across", [P, 2, CHUNK])
        t_across = sb("t_across", [P, CHUNK])
        t = sb("t", [P, 2, BLOCKS, D])
        zeros = ctx.enter_context(nc.sbuf_tensor("zeros", [P, CHUNK], BF16))

        h_acc = ctx.enter_context(nc.psum_tensor("h_acc", [P, GROUPS, CHUNK], F32))
        t_acc = ctx.enter_context(nc.psum_tensor("t_acc", [P, CHUNK], F32))
        turn = ctx.enter_context(nc.psum_tensor("turn", [P, 2, CHUNK], F32))

        s_diag = sem("s_diag")
        s_vectors = sem("s_vectors")
        s_w = sem("s_w")
        s_turned = [[sem(f"s_turned{a}{m}") for m in range(GROUPS)] for a in range(2)]
        s_direct = [sem(f"s_direct{m}") for m in range(GROUPS)]
        s_cols = [sem(f"s_cols{m}") for m in range(GROUPS)]
        s_x = s_cols
        s_eps = sem("s_eps")
        s_zero = sem("s_zero")
        s_ident = sem("s_ident")
        s_centre_part = sem("s_centre_part")
        s_centre = sem("s_centre")
        s_sum = sem("s_sum")
        s_mean = sem("s_mean")
        s_centred = sem("s_centred")
        s_squares = sem("s_squares")
        s_var = sem("s_var")
        s_std = sem("s_std")
        s_rstd = sem("s_rstd")
        s_scale = sem("s_scale")
        s_h = sem("s_h")
        s_dh = sem("s_dh")
        s_dh_across = sem("s_dh_across")
        s_dh_copied = sem("s_dh_copied")
        s_dhw = sem("s_dhw")
        s_dhw_copied = sem("s_dhw_copied")
        s_dhw_back = sem("s_dhw_back")
        s_e = sem("s_e")
        s_res_part = sem("s_res_part")
        s_res = sem("s_res")
        s_first_done = sem("s_first_done")
        s_group_done = sem("s_group_done")
        s_turn_full = [sem(f"s_turn_full{b}") for b in range(2)]
        s_turn_kept = [sem(f"s_turn_kept{b}") for b in range(2)]
        s_t_across = sem("s_t_across")
        s_t_back = sem("s_t_back")
        s_t = sem("s_t")
        s_o_across = sem("s_o_across")
        s_o_centred = sem("s_o_centred")
        s_o_gamma = sem("s_o_gamma")
        s_o_scaled = sem("s_o_scaled")
        s_o_done = sem("s_o_done")
        s_out = sem("s_out")

        def middle_steps(eng, step):
            with eng.Fori(0, PANELS // 2 - 1) as i:
                step(2 * i + 1, 1, i)
                step(2 * i + 2, 0, i + 1)

        def turned_groups(g):
            return LAST_TURNED if isinstance(g, int) and g == LAST else list(range(GROUPS))

        def turns_before(g, m):
            return TURNS * g + BLOCKS // 2 * (len(FIRST_BOTH) + turned_groups(g).index(m))

        def turns_before_0(m, chunk):
            return BLOCKS // 2 * (m + chunk + sum(n < m for n in FIRST_BOTH))

        def cols_loads(g, m):
            return g + 1 + (m not in FIRST_BOTH)

        def turned_loads(a, half):
            return half + 2 * a

        def turned_into_0(m, chunk, b):
            return (turned[:, 0, m, :, P * b:P * (b + 1)], cols[:, m, b].rearrange("p (k r) -> p k r", k=BLOCKS))[chunk]

        def rows_of(m):
            return slice(GT * m, GT * (m + 1))

        def by_tile(v, d=D):
            return v.unsqueeze(2).to_broadcast([P, GT, d])

        block = ctx.enter_context(nc.Block())

        @block.sync
        def _(sp):
            sp.dma_start(xs[:, 0:GT, :], x[:, 0:GT, :]).then_inc(s_x[0], 16)
            sp.dma_start(diag_s[:], diag).then_inc(s_diag, 16)
            for n, v in enumerate((par_u, par_i)):
                sp.dma_start(par[:, n, :], v.partition_broadcast(P)).then_inc(s_diag, 16)

            def load(where, what, signal):
                sp.dma_start(where.rearrange("p b c -> p (b c)"), what).then_inc(signal, 16)

            def load_cols(g, m):
                load(cols[:, m], adj_cols[g, m], s_cols[m])

            def step(g, a):
                for m in range(GROUPS):
                    sp.wait_ge(s_group_done, GROUPS * (g - 1) + m + 1)
                    load(turned[:, a, m], adj_rows[g, m, 0], s_turned[a][m])
                    load(direct[:, m], adj_rows[g, m, 1], s_direct[m])
                    if not (isinstance(g, int) and g == 1 and m in FIRST_BOTH):
                        load_cols(g - 1, m)

            for m in range(GROUPS):
                load(turned[:, 1, m], adj_rows[0, m, 0], s_turned[1][m])
                load(direct[:, m], adj_rows[0, m, 1], s_direct[m])
            step(1, 1)
            with sp.Fori(1, PANELS // 2) as i:
                step(2 * i, 0)
                step(2 * i + 1, 1)
            for m in range(GROUPS):
                sp.wait_ge(s_group_done, GROUPS * LAST + m + 1)
                if m in LAST_LOADED:
                    load(turned[:, 0, m], adj_last[LAST_LOADED.index(m)], s_turned[0][m])
                load_cols(LAST, m)
            for m in range(GROUPS):
                sp.wait_ge(s_o_done, m + 1)
                sp.dma_start(out[:, rows_of(m), :], xs[:, rows_of(m), :]).then_inc(s_out, 16)
            sp.wait_ge(s_out, 16 * GROUPS)

        @block.gpsimd
        def _(pool):
            nc.gpsimd.memset(eps[:], LN_EPS).then_inc(s_eps, 1)
            nc.gpsimd.memset(ident[:], 0.0).then_inc(s_zero, 1)
            nc.gpsimd.memset(wdiag[:], 0.0).then_inc(s_zero, 1)
            nc.gpsimd.memset(zeros[:], 0.0).then_inc(s_zero, 1)
            nc.gpsimd.memset(centre[:], 0.0).then_inc(s_zero, 1)
            pool.wait_ge(s_zero, 4)
            nc.gpsimd.affine_select(out=ident[:], in_=ident[:], compare_op=ALU.not_equal, fill=1.0, base=0,
                                    pattern=[[-1, P]], channel_multiplier=1).then_inc(s_ident, 1)
            for m in range(GROUPS):
                if m == 0:
                    pool.wait_ge(s_scale, 2)
                if m >= 2:
                    pool.wait_ge(s_dh_across, m - 1)
                pool.wait_ge(s_h, m + 1)
                nc.gpsimd.tensor_tensor(scaled[:, m % 2], e[:, rows_of(m), :], by_tile(diag_s[:, rows_of(m)]),
                                        ALU.mult).then_inc(s_dh, 1)
                nc.gpsimd.tensor_tensor(xs[:, rows_of(m), :], xs[:, rows_of(m), :], e[:, rows_of(m), :],
                                        ALU.add).then_inc(s_res_part, 1)
            pool.wait_ge(s_vectors, 32)
            for m in range(GROUPS):
                pool.wait_ge(s_res_part, m + 1)
                nc.gpsimd.tensor_tensor(xs[:, rows_of(m), :], xs[:, rows_of(m), :],
                                        beta_s[:].unsqueeze(1).to_broadcast([P, GT, D]),
                                        ALU.add).then_inc(s_res, 1)
            pool.wait_ge(s_res, GROUPS)
            for d in range(2):
                half = slice(D * d, D * (d + 1))
                nc.gpsimd.memset(centre[half, half], -1.0 / D).then_inc(s_centre_part, 1)
            pool.wait_ge(s_centre_part, 2)
            nc.gpsimd.affine_select(out=centre[:], in_=centre[:], compare_op=ALU.not_equal, fill=1.0 - 1.0 / D,
                                    base=0, pattern=[[-1, P]], channel_multiplier=1).then_inc(s_centre, 1)

        @block.scalar
        def _(act):
            for m in range(1, GROUPS):
                act.dma_start(xs[:, GT * m:GT * (m + 1), :], x[:, GT * m:GT * (m + 1), :]).then_inc(s_x[m], 16)
            act.wait_ge(s_zero, 4)
            for n, w in enumerate((w_u, w_i)):
                for d in range(2):
                    act.dma_start(wdiag[D * d:D * (d + 1), n, D * d:D * (d + 1)], w).then_inc(s_w, 16)
            act.dma_start(gamma_s[:], gamma.partition_broadcast(P)).then_inc(s_vectors, 16)
            act.dma_start(beta_s[:], beta.partition_broadcast(P)).then_inc(s_vectors, 16)

            def square(n):
                act.wait_ge(s_centred, n + 1)
                if n >= 2:
                    act.wait_ge(s_var, n - 1)
                nc.scalar.activation(squares[:, n % 2], centred[:, n % 2], ACT.Square).then_inc(s_squares, 1)

            def square_out(m):
                n = GROUPS + m
                act.wait_ge(s_o_centred, m + 1)
                act.wait_ge(s_var, n - 1)
                nc.scalar.activation(squares[:, n % 2], turn[:, m % 2].rearrange("p (k d) -> p k d", d=D),
                                     ACT.Square).then_inc(s_squares, 1)

            def std(n):
                act.wait_ge(s_var, n + 1)
                if n == 0:
                    act.wait_ge(s_eps, 1)
                nc.scalar.activation(var[:, n % 2], var[:, n % 2], ACT.Sqrt, bias=eps[:],
                                     scale=1.0 / D).then_inc(s_std, 1)

            def dh_across(m):
                act.wait_ge(s_dh_across, m + 1)
                if m >= 2:
                    act.wait_ge(s_dhw_back, m - 1)
                nc.scalar.copy(across[:, m % 2], h_acc[:, m]).then_inc(s_dh_copied, 1)

            def dhw_across(m):
                act.wait_ge(s_dhw, m + 1)
                nc.scalar.copy(across[:, m % 2], h_acc[:, m]).then_inc(s_dhw_copied, 1)

            def keep_turn(g, a, m, b):
                act.wait_ge(s_turn_full[b % 2], turns_before(g, m) + b // 2 + 1)
                nc.scalar.copy(turned[:, a, m, :, P * b:P * (b + 1)],
                               turn[:, b % 2].rearrange("p (k r) -> p k r", k=BLOCKS)
                               ).then_inc(s_turn_kept[b % 2], 1)

            def keep_t_across(g):
                act.wait_ge(s_first_done, g + 1)
                nc.scalar.copy(t_across[:], t_acc[:]).then_inc(s_t_across, 1)

            def step(g, a, half):
                for m in range(GROUPS):
                    if m == GROUPS - 1:
                        keep_t_across(g)
                    if m in turned_groups(g):
                        for b in range(1, BLOCKS, 2):
                            keep_turn(g, a, m, b)

            def keep_turn_0(m, chunk, blocks):
                for b in blocks:
                    act.wait_ge(s_turn_full[1], turns_before_0(m, chunk) + b // 2 + 1)
                    nc.scalar.copy(turned_into_0(m, chunk, b), turn[:, 1].rearrange("p (k r) -> p k r", k=BLOCKS)
                                   ).then_inc(s_turn_kept[1], 1)

            square(0)
            square(1)
            std(0)
            keep_turn_0(0, 0, (1,))
            dh_across(0)
            square(2)
            std(1)
            keep_turn_0(0, 0, (3,))
            dhw_across(0)
            if 0 in FIRST_BOTH:
                keep_turn_0(0, 1, (1, 3))
            for m in range(GROUPS):
                if m + 3 < GROUPS:
                    square(m + 3)
                if m + 2 < GROUPS:
                    std(m + 2)
                if m + 1 < GROUPS:
                    dh_across(m + 1)
                    keep_turn_0(m + 1, 0, (1, 3))
                    dhw_across(m + 1)
                    if m + 1 in FIRST_BOTH:
                        keep_turn_0(m + 1, 1, (1, 3))
            keep_t_across(0)
            middle_steps(act, step)
            step(LAST, LAST % 2, LAST // 2)
            for m in range(GROUPS):
                act.wait_ge(s_group_done, GROUPS * PANELS + m + 1)
                if m >= 2:
                    act.wait_ge(s_o_centred, m - 1)
                nc.scalar.copy(across[:, m % 2], h_acc[:, m]).then_inc(s_o_across, 1)
                square_out(m)
                std(GROUPS + m)

        @block.vector
        def _(dve):
            def centre_rows(n, source):
                nc.vector.tensor_reduce(mean[:, n % 2], source, AX.X, ALU.add).then_inc(s_sum, 1)
                dve.wait_ge(s_sum, n + 1)
                nc.vector.tensor_scalar(mean[:, n % 2], mean[:, n % 2], 1.0 / D, None, ALU.mult).then_inc(s_mean, 1)
                dve.wait_ge(s_mean, n + 1)
                nc.vector.tensor_tensor(centred[:, n % 2], source, by_tile(mean[:, n % 2]),
                                        ALU.subtract).then_inc(s_centred, 1)

            def sum_squares(n):
                dve.wait_ge(s_squares, n + 1)
                nc.vector.tensor_reduce(var[:, n % 2], squares[:, n % 2], AX.X, ALU.add).then_inc(s_var, 1)

            def inverse_deviation(n):
                dve.wait_ge(s_std, n + 1)
                nc.vector.reciprocal(rstd[:, n % 2], var[:, n % 2]).then_inc(s_rstd, 1)
                dve.wait_ge(s_rstd, n + 1)
                return by_tile(rstd[:, n % 2])

            def centre_x(m):
                dve.wait_ge(s_x[m], 16)
                centre_rows(m, xs[:, rows_of(m), :])

            def layer_input(m):
                sum_squares(m)
                r = inverse_deviation(m)
                nc.vector.scalar_tensor_tensor(e[:, rows_of(m), :], centred[:, m % 2], 0.0, r,
                                               ALU.max, ALU.mult).then_inc(s_h, 1)

            def embed(m):
                dve.wait_ge(s_dhw_back, m + 1)
                dve.wait_ge(s_res_part, m + 1)
                nc.vector.tensor_tensor(e[:, rows_of(m), :], h_acc[:, m].rearrange("p (k d) -> p k d", d=D),
                                        e[:, rows_of(m), :], ALU.add).then_inc(s_e, 1)

            def keep_turn(g, a, m, b):
                dve.wait_ge(s_turn_full[0], turns_before(g, m) + b // 2 + 1)
                nc.vector.tensor_copy(turned[:, a, m, :, P * b:P * (b + 1)],
                                      turn[:, 0].rearrange("p (k r) -> p k r", k=BLOCKS)
                                      ).then_inc(s_turn_kept[0], 1)

            def keep_turn_0(m, chunk):
                for b in (0, 2):
                    dve.wait_ge(s_turn_full[0], turns_before_0(m, chunk) + b // 2 + 1)
                    nc.vector.tensor_copy(turned_into_0(m, chunk, b),
                                          turn[:, 0].rearrange("p (k r) -> p k r", k=BLOCKS)
                                          ).then_inc(s_turn_kept[0], 1)

            def keep_t(g, a):
                dve.wait_ge(s_t_back, g + 1)
                nc.vector.tensor_reduce(t[:, a], t_acc[:].rearrange("p (b s d) -> p b d s", b=BLOCKS, s=2),
                                        AX.X, ALU.add).then_inc(s_t, 1)

            def step(g, a, half):
                for m in range(GROUPS):
                    if m in turned_groups(g):
                        keep_turn(g, a, m, 0)
                    if m == GROUPS - 1:
                        keep_t(g, a)
                    if m in turned_groups(g):
                        keep_turn(g, a, m, 2)

            centre_x(0)
            dve.wait_ge(s_diag, 48)
            for n, (lo, hi) in enumerate(((0, N_USERS // P), (N_USERS // P, TILES))):
                nc.vector.tensor_scalar(diag_s[:, lo:hi], diag_s[:, lo:hi], par[:, n, 0:1], par[:, n, 1:2],
                                        ALU.mult, ALU.mult).then_inc(s_scale, 1)
            for m in range(1, GROUPS + 2):
                if m < GROUPS:
                    centre_x(m)
                if m <= GROUPS:
                    layer_input(m - 1)
                if m >= 2:
                    keep_turn_0(m - 2, 0)
                    embed(m - 2)
                    if m - 2 in FIRST_BOTH:
                        keep_turn_0(m - 2, 1)
            keep_t(0, 0)
            middle_steps(dve, step)
            step(LAST, LAST % 2, LAST // 2)
            gamma_rows = gamma_s[:].unsqueeze(1).to_broadcast([P, GT, D])
            for m in range(GROUPS):
                n = GROUPS + m
                sum_squares(n)
                if m == 0:
                    dve.wait_ge(s_vectors, 32)
                nc.vector.tensor_tensor(scaled[:, m % 2], turn[:, m % 2].rearrange("p (k d) -> p k d", d=D),
                                        gamma_rows, ALU.mult).then_inc(s_o_gamma, 1)
                r = inverse_deviation(n)
                dve.wait_ge(s_o_gamma, m + 1)
                nc.vector.tensor_tensor(scaled[:, m % 2], scaled[:, m % 2], r, ALU.mult).then_inc(s_o_scaled, 1)
                dve.wait_ge(s_o_scaled, m + 1)
                dve.wait_ge(s_res, m + 1)
                res = xs[:, rows_of(m), :].rearrange("p (s b) d -> p b s d", s=2)
                nc.vector.tensor_tensor(res, scaled[:, m % 2].rearrange("p (b s) d -> p b s d", s=2), res,
                                        ALU.add).then_inc(s_o_done, 1)

        @block.tensor
        def _(pe):
            def dh_turn(m):
                if m == 0:
                    pe.wait_ge(s_ident, 1)
                pe.wait_ge(s_dh, m + 1)
                for b in range(BLOCKS):
                    last = nc.tensor.transpose(h_acc[:, m, P * b:P * (b + 1)],
                                               scaled[:, m % 2, 2 * b:2 * b + 2, :].rearrange("p k d -> p (k d)"),
                                               ident[:])
                last.then_inc(s_dh_across, 1)

            def dh_weights(m):
                if m == 0:
                    pe.wait_ge(s_w, 64)
                pe.wait_ge(s_dh_copied, m + 1)
                nc.tensor.matmul(h_acc[:, m], wdiag[:, int(m >= USER_GROUPS)], across[:, m % 2],
                                 start=True, stop=True).then_inc(s_dhw, 1)

            def dhw_turn(m):
                pe.wait_ge(s_dhw_copied, m + 1)
                for b in range(BLOCKS):
                    last = nc.tensor.transpose(h_acc[:, m, P * b:P * (b + 1)],
                                               across[:, m % 2, P * b:P * (b + 1)], ident[:])
                last.then_inc(s_dhw_back, 1)

            def clear(m):
                pe.wait_ge(s_e, m + 1)
                nc.tensor.matmul(h_acc[:, m], zeros[:, 0:P], zeros[:], start=True, stop=False,
                                 skip_group_check=True)

            def first(g, buffer, loads, m):
                pe.wait_ge(s_turned[buffer][m], 16 * loads)
                pe.wait_ge(s_direct[m], 16 * (g + 1))
                for k in range(BLOCKS):
                    for s, rows in enumerate((turned[:, buffer, m, k], direct[:, m, k])):
                        last = nc.tensor.matmul(t_acc[D * s:D * (s + 1), :], e[:, GT * m + BLOCKS * s + k, :], rows,
                                                start=(m == 0 and k == 0),
                                                stop=(m == GROUPS - 1 and k == BLOCKS - 1))
                if m == GROUPS - 1:
                    last.then_inc(s_first_done, 1)
                return last

            def turn_block(rows, b):
                for k in range(BLOCKS):
                    last = nc.tensor.transpose(turn[:, b % 2, P * k:P * (k + 1)], rows[:, k, P * b:P * (b + 1)],
                                               ident[:])
                last.then_inc(s_turn_full[b % 2], 1)

            def turn_blocks(g, a, m, blocks):
                for b in blocks:
                    pe.wait_ge(s_turn_kept[b % 2], turns_before(g, m) + b // 2)
                    turn_block(turned[:, a, m], b)

            def turn_blocks_0(m, chunk, blocks):
                if 0 in blocks:
                    pe.wait_ge((s_turned[1][m], s_direct[m])[chunk], 16)
                for b in blocks:
                    before = turns_before_0(m, chunk) + b // 2
                    if before:
                        pe.wait_ge(s_turn_kept[b % 2], before)
                    turn_block((turned[:, 1, m], direct[:, m])[chunk], b)

            def second_waits(g, m):
                pe.wait_ge(s_cols[m], 16 * cols_loads(g, m))
                if m in turned_groups(g):
                    for b in range(2):
                        pe.wait_ge(s_turn_kept[b], turns_before(g, m) + 2)
                else:
                    pe.wait_ge(s_turned[0][m], 16 * (turned_loads(0, LAST // 2) + 1))
                if m == 0:
                    pe.wait_ge(s_t, g + 1)

            def second(g, a, m, blocks):
                for b in blocks:
                    if m in turned_groups(g):
                        chunk0 = turned[:, a, m, :, P * b:P * (b + 1)]
                    else:
                        chunk0 = turned[:, 0, m, b]
                    for s, rows in enumerate((chunk0, cols[:, m, b])):
                        last = nc.tensor.matmul(h_acc[D * s:D * (s + 1), m], t[:, a, b, :], rows, start=False,
                                                stop=(isinstance(g, int) and g == LAST and b == BLOCKS - 1),
                                                skip_group_check=True)
                return last

            def t_turn(g):
                pe.wait_ge(s_t_across, g + 1)
                for b in range(BLOCKS):
                    last = nc.tensor.transpose(t_acc[:, P * b:P * (b + 1)], t_across[:, P * b:P * (b + 1)], ident[:])
                    if isinstance(g, int) and g == 0 and b == 0:
                        last.then_inc(s_group_done, 1)
                last.then_inc(s_t_back, 1)

            def step(g, a, half):
                for m in range(GROUPS):
                    if m == 0:
                        pe.wait_ge(s_t, g)
                    first(g, a, turned_loads(a, half), m)
                    turns = m in turned_groups(g)
                    if turns:
                        turn_blocks(g, a, m, (0, 1))
                    second_waits(g - 1, m)
                    second(g - 1, 1 - a, m, (0, 1))
                    if m == GROUPS - 1:
                        t_turn(g)
                    if turns:
                        turn_blocks(g, a, m, (2, 3))
                    second(g - 1, 1 - a, m, (2, 3)).then_inc(s_group_done, 1)

            def out_turn(m):
                if m == 0:
                    pe.wait_ge(s_centre, 1)
                pe.wait_ge(s_o_across, m + 1)
                if m >= 2:
                    pe.wait_ge(s_squares, GROUPS + m - 1)
                    pe.wait_ge(s_o_gamma, m - 1)
                else:
                    pe.wait_ge(s_turn_kept[m], TURNS * LAST + BLOCKS // 2 * (len(FIRST_BOTH) + len(LAST_TURNED)))
                for b in range(BLOCKS):
                    last = nc.tensor.matmul(turn[:, m % 2, P * b:P * (b + 1)],
                                            across[:, m % 2, P * b:P * (b + 1)], centre[:], start=True, stop=True)
                last.then_inc(s_o_centred, 1)

            pe.wait_ge(s_ident, 1)
            turn_blocks_0(0, 0, range(2))
            dh_turn(0)
            turn_blocks_0(0, 0, range(2, BLOCKS))
            dh_weights(0)
            dhw_turn(0)
            if 0 in FIRST_BOTH:
                turn_blocks_0(0, 1, range(BLOCKS))
            for m in range(GROUPS):
                clear(m)
                last = first(0, 1, 1, m)
                if m + 1 < GROUPS:
                    last.then_inc(s_group_done, 1)
                    dh_turn(m + 1)
                    turn_blocks_0(m + 1, 0, range(BLOCKS))
                    dh_weights(m + 1)
                    dhw_turn(m + 1)
                    if m + 1 in FIRST_BOTH:
                        turn_blocks_0(m + 1, 1, range(BLOCKS))
            t_turn(0)
            middle_steps(pe, step)
            step(LAST, LAST % 2, LAST // 2)
            for m in range(GROUPS):
                second_waits(LAST, m)
                second(LAST, LAST % 2, m, (0, 1))
                if m >= 1:
                    out_turn(m - 1)
                second(LAST, LAST % 2, m, (2, 3)).then_inc(s_group_done, 1)
            out_turn(GROUPS - 1)


def kernel(x, adj, L0_gnn_W_u, L0_gnn_diag_u, L0_gnn_par_u, L0_gnn_W_i, L0_gnn_diag_i, L0_gnn_par_i,
           L0_gnn_ln_gamma, L0_gnn_ln_beta):
    import concourse.bacc as bacc
    import numpy as np
    from concourse.bass_utils import run_bass_kernel_spmd

    def tiles(v):
        v = np.asarray(v)
        return np.ascontiguousarray(np.swapaxes(v.reshape(TILES, P, *v.shape[1:]), 0, 1))

    by_rows = np.asarray(adj).reshape(GROUPS, 2, BLOCKS, P, PANELS, CHUNK)
    by_cols = np.asarray(adj).reshape(GROUPS, 2, CHUNK, PANELS, BLOCKS, P)[:, 1]
    last_by_cols = np.asarray(adj).reshape(GROUPS, 2, CHUNK, PANELS, BLOCKS, P)[:, 0, :, LAST]
    arrays = {
        "x": tiles(x),
        "adj_rows": np.ascontiguousarray(by_rows.transpose(4, 0, 1, 3, 2, 5)).reshape(
            PANELS, GROUPS, 2, P, BLOCKS * CHUNK),
        "adj_cols": np.ascontiguousarray(by_cols.transpose(2, 0, 4, 3, 1)).reshape(
            PANELS, GROUPS, P, BLOCKS * CHUNK),
        "adj_last": np.ascontiguousarray(last_by_cols[list(LAST_LOADED)].transpose(0, 3, 2, 1)).reshape(
            len(LAST_LOADED), P, BLOCKS * CHUNK),
        "w_u": np.asarray(L0_gnn_W_u),
        "w_i": np.asarray(L0_gnn_W_i),
        "diag": tiles(np.concatenate([np.asarray(L0_gnn_diag_u), np.asarray(L0_gnn_diag_i)])),
        "par_u": np.asarray(L0_gnn_par_u),
        "par_i": np.asarray(L0_gnn_par_i),
        "gamma": np.asarray(L0_gnn_ln_gamma),
        "beta": np.asarray(L0_gnn_ln_beta),
    }
    nc = bacc.Bacc("TRN2", target_bir_lowering=False, num_devices=1)
    ins = [nc.dram_tensor(name, a.shape, F32, kind="ExternalInput").ap() for name, a in arrays.items()]
    out = nc.dram_tensor("out", (P, TILES, D), F32, kind="ExternalOutput").ap()
    gnn_layer(nc, *ins, out)
    got = run_bass_kernel_spmd(nc, [arrays], core_ids=[0]).results[0]["out"]
    return np.ascontiguousarray(np.swapaxes(got, 0, 1)).reshape(N, D)
```
